# Optimizing a Trainium2 kernel written in Bass

```python
import numpy as np
import jax
import jax.numpy as jnp

def _softmax(x, axis=-1):
    return jax.nn.softmax(x, axis=axis)
def _gelu(x):
    return jax.nn.gelu(x, approximate=True)
def _silu(x):
    return jax.nn.silu(x)
def _sigmoid(x):
    return jax.nn.sigmoid(x)
def _layernorm(x, axis=-1, eps=1e-5):
    m = jnp.mean(x, axis=axis, keepdims=True)
    v = jnp.var(x, axis=axis, keepdims=True)
    return (x - m) / jnp.sqrt(v + eps)
def _scatter_add(tgt, idx, src, axis=0):
    return tgt.at[idx].add(src)
def _segment_sum(src, seg, n):
    return jax.ops.segment_sum(src, seg, n)

kernel_name = 'mk_conv_seq_d1_conv_nchw512_5e5380'

def setup_inputs(seed: int = 0):
    np.random.seed(seed)
    _w = jnp.asarray
    def _rec_inputs():
        import jax
        import jax.numpy as jnp
        _gk = jax.random.key(seed)
        x = -0.0003929 + 0.9999 * jax.random.normal(jax.random.fold_in(_gk, 1), (8, 512, 64, 64), jnp.float32)
        return x
    x = _rec_inputs()
    def _L0_conv_setup():
        import jax, jax.numpy as jnp
        import numpy as np
        PSP_SIZES = (1, 3, 6, 8)
        EPS = 1e-05

        def _adaptive_max_pool_flat(x, s):
            B, C, H, W = x.shape
            hs = [int(np.floor(i * H / s)) for i in range(s)]
            he = [int(np.ceil((i + 1) * H / s)) for i in range(s)]
            ws = [int(np.floor(j * W / s)) for j in range(s)]
            we = [int(np.ceil((j + 1) * W / s)) for j in range(s)]
            cells = []
            for i in range(s):
                for j in range(s):
                    cells.append(jnp.max(x[:, :, hs[i]:he[i], ws[j]:we[j]], axis=(2, 3)))
            return jnp.stack(cells, axis=-1)

        def _psp(x):
            return jnp.concatenate([_adaptive_max_pool_flat(x, s) for s in PSP_SIZES], axis=-1)

        def _conv1x1(x, w):
            return jnp.einsum('bchw,oc->bohw', x, w)

        def _bn(y, gamma, beta, mean, var):
            inv = jax.lax.rsqrt(var + EPS)
            return (y - mean[None, :, None, None]) * (gamma * inv)[None, :, None, None] + beta[None, :, None, None]
        key = jax.random.key(seed)
        ks = jax.random.split(key, 4)
        B, Cin, H, W = (8, 512, 64, 64)
        Ck, Cv = (256, 512)
        x = jax.random.normal(ks[0], (B, Cin, H, W), dtype=jnp.float32)
        qk_w = jax.random.normal(ks[1], (Ck, Cin), dtype=jnp.float32) * 0.02
        v_w = jax.random.normal(ks[2], (Cv, Cin), dtype=jnp.float32) * 0.02
        out_w = jax.random.normal(ks[3], (Cin, Cv), dtype=jnp.float32) * 0.02
        return {'x': x, 'qk_w': qk_w, 'qk_gamma': jnp.ones(Ck), 'qk_beta': jnp.zeros(Ck), 'qk_mean': jnp.zeros(Ck), 'qk_var': jnp.ones(Ck), 'v_w': v_w, 'v_gamma': jnp.ones(Cv), 'v_beta': jnp.zeros(Cv), 'v_mean': jnp.zeros(Cv), 'v_var': jnp.ones(Cv), 'out_w': out_w, 'out_gamma': jnp.ones(Cin), 'out_beta': jnp.zeros(Cin), 'out_mean': jnp.zeros(Cin), 'out_var': jnp.ones(Cin)}
    _L0_conv_all = _L0_conv_setup()
    _L0_conv_in = {k: v for k, v in _L0_conv_all.items() if k in ('qk_w', 'qk_gamma', 'qk_beta', 'qk_mean', 'qk_var', 'v_w', 'v_gamma', 'v_beta', 'v_mean', 'v_var', 'out_w', 'out_gamma', 'out_beta', 'out_mean', 'out_var', )}
    del _L0_conv_all

    return {
        "x": x,
        "L0_conv_qk_w": _L0_conv_in["qk_w"],
        "L0_conv_qk_gamma": _L0_conv_in["qk_gamma"],
        "L0_conv_qk_beta": _L0_conv_in["qk_beta"],
        "L0_conv_qk_mean": _L0_conv_in["qk_mean"],
        "L0_conv_qk_var": _L0_conv_in["qk_var"],
        "L0_conv_v_w": _L0_conv_in["v_w"],
        "L0_conv_v_gamma": _L0_conv_in["v_gamma"],
        "L0_conv_v_beta": _L0_conv_in["v_beta"],
        "L0_conv_v_mean": _L0_conv_in["v_mean"],
        "L0_conv_v_var": _L0_conv_in["v_var"],
        "L0_conv_out_w": _L0_conv_in["out_w"],
        "L0_conv_out_gamma": _L0_conv_in["out_gamma"],
        "L0_conv_out_beta": _L0_conv_in["out_beta"],
        "L0_conv_out_mean": _L0_conv_in["out_mean"],
        "L0_conv_out_var": _L0_conv_in["out_var"],
    }

def reference(x, L0_conv_qk_w, L0_conv_qk_gamma, L0_conv_qk_beta, L0_conv_qk_mean, L0_conv_qk_var, L0_conv_v_w, L0_conv_v_gamma, L0_conv_v_beta, L0_conv_v_mean, L0_conv_v_var, L0_conv_out_w, L0_conv_out_gamma, L0_conv_out_beta, L0_conv_out_mean, L0_conv_out_var):
    import jax
    import jax.numpy as jnp
    def _L0_conv_ref(x, qk_w, qk_gamma, qk_beta, qk_mean, qk_var, v_w, v_gamma, v_beta, v_mean, v_var, out_w, out_gamma, out_beta, out_mean, out_var):
        import jax, jax.numpy as jnp
        import numpy as np
        PSP_SIZES = (1, 3, 6, 8)
        EPS = 1e-05

        def _adaptive_max_pool_flat(x, s):
            B, C, H, W = x.shape
            hs = [int(np.floor(i * H / s)) for i in range(s)]
            he = [int(np.ceil((i + 1) * H / s)) for i in range(s)]
            ws = [int(np.floor(j * W / s)) for j in range(s)]
            we = [int(np.ceil((j + 1) * W / s)) for j in range(s)]
            cells = []
            for i in range(s):
                for j in range(s):
                    cells.append(jnp.max(x[:, :, hs[i]:he[i], ws[j]:we[j]], axis=(2, 3)))
            return jnp.stack(cells, axis=-1)

        def _psp(x):
            return jnp.concatenate([_adaptive_max_pool_flat(x, s) for s in PSP_SIZES], axis=-1)

        def _conv1x1(x, w):
            return jnp.einsum('bchw,oc->bohw', x, w)

        def _bn(y, gamma, beta, mean, var):
            inv = jax.lax.rsqrt(var + EPS)
            return (y - mean[None, :, None, None]) * (gamma * inv)[None, :, None, None] + beta[None, :, None, None]
        B, Cin, H, W = x.shape
        Ck = qk_w.shape[0]
        Cv = v_w.shape[0]
        qk = jax.nn.relu(_bn(_conv1x1(x, qk_w), qk_gamma, qk_beta, qk_mean, qk_var))
        val = jax.nn.relu(_bn(_conv1x1(x, v_w), v_gamma, v_beta, v_mean, v_var))
        key = _psp(qk)
        value = _psp(val).transpose(0, 2, 1)
        query = qk.reshape(B, Ck, H * W).transpose(0, 2, 1)
        scores = jnp.einsum('bnc,bcs->bns', query, key) * Ck ** (-0.5)
        scores = jax.nn.softmax(scores, axis=-1)
        y = jnp.einsum('bns,bsc->bnc', scores, value)
        y = y.transpose(0, 2, 1).reshape(B, Cv, H, W)
        y = _bn(_conv1x1(y, out_w), out_gamma, out_beta, out_mean, out_var)
        return x + y

    def _gn(v, G=32, eps=1e-5):
        B_, C_, H_, W_ = v.shape
        g = v.reshape(B_, G, C_ // G, H_, W_)
        m = jnp.mean(g, axis=(2, 3, 4), keepdims=True)
        s = jnp.var(g, axis=(2, 3, 4), keepdims=True)
        return ((g - m) / jnp.sqrt(s + eps)).reshape(v.shape)

    def _ln_c(v, eps=1e-6):
        m = jnp.mean(v, axis=1, keepdims=True)
        s = jnp.var(v, axis=1, keepdims=True)
        return (v - m) / jnp.sqrt(s + eps)

    def _ln_t(v, eps=1e-5):
        m = jnp.mean(v, axis=-1, keepdims=True)
        s = jnp.var(v, axis=-1, keepdims=True)
        return (v - m) / jnp.sqrt(s + eps)

    def _to_tokens(v):
        B_, C_, H_, W_ = v.shape
        return v.reshape(B_, C_, H_ * W_).transpose(0, 2, 1)
    def _from_tokens(t, like):
        B_, C_, H_, W_ = like.shape
        return t.transpose(0, 2, 1).reshape(B_, C_, H_, W_)

    x = _L0_conv_ref(x, L0_conv_qk_w, L0_conv_qk_gamma, L0_conv_qk_beta, L0_conv_qk_mean, L0_conv_qk_var, L0_conv_v_w, L0_conv_v_gamma, L0_conv_v_beta, L0_conv_v_mean, L0_conv_v_var, L0_conv_out_w, L0_conv_out_gamma, L0_conv_out_beta, L0_conv_out_mean, L0_conv_out_var)
    return x


_drawn_inputs = setup_inputs


def setup_inputs(seed=0):
    import zlib

    import numpy as np

    out = dict(_drawn_inputs(seed))
    spreads = {'L0_conv_qk_gamma': (1.0, 0.6),
     'L0_conv_qk_beta': (0.0, 0.8),
     'L0_conv_qk_mean': (0.0, 0.8),
     'L0_conv_qk_var': (1.0, 0.6),
     'L0_conv_v_gamma': (1.0, 0.2),
     'L0_conv_v_beta': (0.0, 0.437),
     'L0_conv_v_mean': (0.0, 0.407),
     'L0_conv_v_var': (1.0, 0.2),
     'L0_conv_out_gamma': (1.0, 0.2),
     'L0_conv_out_beta': (0.0, 0.1),
     'L0_conv_out_mean': (0.0, 0.1),
     'L0_conv_out_var': (1.0, 0.2)}
    factors = {'L0_conv_qk_w': 8.0, 'L0_conv_v_w': 2.672}
    for name, (base, spread) in spreads.items():
        noise = np.random.default_rng([zlib.crc32(name.encode()), seed]).standard_normal(out[name].shape)
        drawn = base * np.exp(spread * noise) if base else spread * noise
        out[name] = jnp.asarray(drawn.astype(out[name].dtype))
    for name, factor in factors.items():
        out[name] = (out[name] * factor).astype(out[name].dtype)
    return out
```

```python
from contextlib import ExitStack

import concourse.bass as bass
from concourse import mybir
from concourse.alu_op_type import AluOpType as ALU

F32 = mybir.dt.float32
F32R = mybir.dt.float32r
ACT = mybir.ActivationFunctionType
AX = mybir.AxisListType

P = 128
EPS = 1e-5
CELL1, CELL3, CELL6, CELL8 = 0, 1, 1 + 9, 1 + 9 + 36
CELLS = 1 + 9 + 36 + 64
WINDOWS6 = [(0, 11), (10, 12), (21, 11)]
ROW_PARTS = [[(0, 8)], [(0, 3), (2, 8)], [(0, 6), (5, 8)], [(0, 8)]]
PART_AT = [0, 1, 3, 5, 6, 7, 9, 11]


def psp_attention(nc, x, qk_w, qk_bn, v_w, v_bn, out_w, out_bn, out):
    B, CIN, H, W = x.shape
    CK, CV = qk_w.shape[0], v_w.shape[0]
    NT = 8
    TN = H * W // NT
    KC = CIN // P
    VC, QC, OC = CV // P, CK // P, CIN // P
    CC = VC + QC
    SUB = TN // P
    GR = 4
    RING = 3
    assert (H, W, TN, KC, VC, QC) == (64, 64, 512, 4, 4, 2)
    PAR = CC + OC

    x_v = x.rearrange("b (k p) h w -> b p k (h w)", p=P)
    out_v = out.rearrange("b (k p) h w -> b p k (h w)", p=P)

    with ExitStack() as ctx:
        def sb(name, shape, dt=F32):
            return ctx.enter_context(nc.sbuf_tensor(name, shape, dt))

        def psum(name):
            return ctx.enter_context(nc.psum_tensor(name, [P, TN], F32))

        def sem(name):
            return ctx.enter_context(nc.semaphore(name))

        xr = sb("xr", [P, RING, GR, KC, TN])
        q = sb("q", [P, NT, QC, TN])
        w_raw = q[:, :, :, :].rearrange("p t c n -> p (t c) n")
        xh_a = sb("xh_a", [P, 2, 2, TN], F32R)
        xl_a = sb("xl_a", [P, 2, 2, TN], F32R)
        xh_b = sb("xh_b", [P, 2, TN], F32R)
        xl_b = sb("xl_b", [P, 2, TN], F32R)
        wh = sb("wh", [P, KC, CC * P], F32R)
        wl = sb("wl", [P, KC, CC * P], F32R)
        woT = sb("woT", [P, VC, CIN])
        row_max = sb("row_max", [P, CC, 2, W])
        part6 = sb("part6", [P, CC, 12, 6])
        rows3 = sb("rows3", [P, CC, 3, 6])
        cells = sb("cells", [P, CC, CELLS])
        key = sb("key", [P, QC, CELLS])
        value = sb("value", [P, VC, CELLS])
        vo_h = sb("vo_h", [CELLS, CIN], F32R)
        vo_l = sb("vo_l", [CELLS, CIN], F32R)
        neg_max = sb("neg_max", [P, SUB])
        sums = sb("sums", [P, SUB])
        rsum = sb("rsum", [P, SUB])
        probs = sb("probs", [P, SUB, CELLS])
        pt_h = sb("pt_h", [CELLS, TN], F32R)
        pt_l = sb("pt_l", [CELLS, TN], F32R)
        ident = sb("ident", [P, P])
        bn_rows = sb("bn_rows", [4 * PAR, P])
        bn = sb("bn", [P, 4, PAR])
        rstd = sb("rstd", [P, PAR])
        tmp = sb("tmp", [P, PAR])
        scale = sb("scale", [P, PAR])
        shift = sb("shift", [P, PAR])

        conv_ps = [psum(f"conv_ps{i}") for i in range(4)]
        score_ps = psum("score_ps")
        t_ps = psum("t_ps")
        out_ps = [psum(f"out_ps{i}") for i in range(2)]

        x_in = [sem(f"x_in{t}") for t in range(NT)]
        y_out = [sem(f"y_out{t}") for t in range(NT)]
        bn_in = sem("bn_in")
        w_in = [sem(f"w_in{i}") for i in range(3)]
        ident_made = sem("ident_made")
        bn_turned = sem("bn_turned")
        bn_step = sem("bn_step")
        sqrt_made = sem("sqrt_made")
        w_scaled = sem("w_scaled")
        w_turned = sem("w_turned")
        w_hi = sem("w_hi")
        w_lo = sem("w_lo")
        x_hi = sem("x_hi")
        x_lo = sem("x_lo")
        conv_done = sem("conv_done")
        late_used = sem("late_used")
        q_stored = sem("q_stored")
        rows_pooled = sem("rows_pooled")
        cells_pooled = sem("cells_pooled")
        grid_step = sem("grid_step")
        key_ready = sem("key_ready")
        value_ready = sem("value_ready")
        scores_done = sem("scores_done")
        max_ready = sem("max_ready")
        exp_done = sem("exp_done")
        rsum_ready = sem("rsum_ready")
        probs_ready = sem("probs_ready")
        turned = sem("turned")
        pt_hi = sem("pt_hi")
        pt_lo = sem("pt_lo")
        vo_done = sem("vo_done")
        vo_hi = sem("vo_hi")
        vo_lo = sem("vo_lo")
        out_done = sem("out_done")
        out_added = sem("out_added")

        block = ctx.enter_context(nc.Block())

        def count(b, t, per, n):
            return b * (NT * per) + (t * per + n)

        def wait(eng, s, b, t, per, n):
            if not isinstance(b, int) or count(b, t, per, n) > 0:
                eng.wait_ge(s, count(b, t, per, n))

        def slot(b, t):
            return (2 * b + (t // GR) % RING) % RING, t % GR

        def scored(b, t):
            return not isinstance(b, int) or (b >= 1 and NT * b + t < NT * (B + 1))

        def output(b, t):
            return not isinstance(b, int) or NT * b + t >= NT + 1

        def convolved(b):
            return not isinstance(b, int) or b < B

        def steps(eng, step):
            for s in range(NT + 2):
                step(*divmod(s, NT))
            with eng.Fori(1, B - 1) as b:
                for s in range(2, NT + 2):
                    step(b + s // NT, s % NT)
            for s in range((B - 1) * NT + 2, (B + 1) * NT + 1):
                step(*divmod(s, NT))

        def next_tile(b, t):
            return (b, t + 1) if t + 1 < NT else (b + 1, 0)

        def splits(b, t):
            return not isinstance(b, int) or NT * b + t + 1 < NT * B

        @block.sync
        def _(sp):
            def load(b, t, sem_t):
                i, j = slot(b, t)
                bb, tt = (b, t) if t < NT else (b + 1, t - NT)
                sp.dma_start(xr[:, i, j, :, :], x_v[bb, :, :, tt * TN:(tt + 1) * TN]).then_inc(x_in[sem_t], 16)

            for t in range(2):
                load(0, t, t)

            def step(b, t):
                last = isinstance(b, int) and NT * b + t + 2 >= NT * B
                if not last:
                    n = (t + 2) % NT
                    if not isinstance(b, int) or NT * b + t + 2 >= NT:
                        sp.wait_ge(x_in[n], (b + (t + 2) // NT) * 16)
                    if not isinstance(b, int) or NT * b + t >= NT + 2:
                        bb = b - 1 if t >= 2 else b - 2
                        sp.wait_ge(y_out[(t - 2) % NT], (bb + 1) * 16)
                    load(b, t + 2, n)
                if output(b, t):
                    wait(sp, out_added, b, t, OC, OC - (NT + 1) * OC)
                    i, j = slot(b, t - NT - 1)
                    tt = (t - 1) % NT
                    bb = b - 1 if t >= 1 else b - 2
                    sp.dma_start(out_v[bb, :, :, tt * TN:(tt + 1) * TN], xr[:, i, j, :, :]).then_inc(y_out[tt], 16)

            steps(sp, step)
            for t in range(NT):
                sp.wait_ge(y_out[t], B * 16)

        @block.gpsimd
        def _(pool):
            nc.gpsimd.memset(ident[:, :], 0.0).then_inc(ident_made, 1)
            pool.wait_ge(ident_made, 1)
            nc.gpsimd.affine_select(out=ident[:, :], in_=ident[:, :], compare_op=ALU.not_equal, fill=1.0, base=0,
                                    pattern=[[-1, P]], channel_multiplier=1).then_inc(ident_made, 1)

        @block.tensor
        def _(pe):
            pe.wait_ge(ident_made, 2)
            pe.wait_ge(bn_in, 12 * 16)
            nc.tensor.transpose(out_ps[0][:, 0:4 * PAR], bn_rows[:, :], ident[0:4 * PAR, 0:4 * PAR]).then_inc(bn_turned, 1)
            for j in range(PAR):
                pe.wait_ge(w_scaled, j + 1)
                if j >= 4:
                    pe.wait_ge(w_lo, j - 3) if j - 4 < CC else pe.wait_ge(w_hi, j - 3)
                for k in range(KC):
                    last = nc.tensor.transpose(conv_ps[j % 4][:, k * P:(k + 1) * P], w_raw[:, j, k * P:(k + 1) * P],
                                               ident[:, :])
                last.then_inc(w_turned, 1)
            pe.wait_ge(w_lo, CC)
            pe.wait_ge(w_hi, PAR)

            def conv(b, t, c):
                if c < 2:
                    wait(pe, rows_pooled, b, t, CC, c + 3 - CC)
                elif c < 4:
                    wait(pe, q_stored, b, t, QC, c - 1 - QC)
                else:
                    wait(pe, rows_pooled, b, t, CC, c - 3)
                bank = conv_ps[c % 4 if t % 2 == 0 else (c + 2) % 4]
                order = range(KC) if c < CC - 1 else [2, 3, 0, 1]
                for n, k in enumerate(order):
                    if c == 0 and k != 1:
                        wait(pe, x_lo, b, t, 3, max(k, 1))
                    hi = xh_a[:, t % 2, k, :] if k < 2 else xh_b[:, k - 2, :]
                    lo = xl_a[:, t % 2, k, :] if k < 2 else xl_b[:, k - 2, :]
                    cols = slice(c * P, (c + 1) * P)
                    nc.tensor.matmul(bank[:, :], wh[:, k, cols], hi, start=(n == 0), stop=False)
                    nc.tensor.matmul(bank[:, :], wl[:, k, cols], hi, start=False, stop=False)
                    last = nc.tensor.matmul(bank[:, :], wh[:, k, cols], lo, start=False, stop=(n == KC - 1))
                    if c == CC - 1 and k >= 2:
                        last.then_inc(late_used, 1)
                last.then_inc(conv_done, 1)

            def turn_probs(b, t):
                if t == 1:
                    pe.wait_ge(vo_lo, b)
                wait(pe, probs_ready, b, t, 1, 1 - (NT + 1))
                wait(pe, pt_lo, b, t, 1, -(NT + 1))
                for j in range(SUB):
                    last = nc.tensor.transpose(t_ps[0:CELLS, j * P:(j + 1) * P], probs[:, j, :], ident[:, :])
                last.then_inc(turned, 1)

            def project(b, t, m):
                if m == 0:
                    wait(pe, pt_lo, b, t, 1, 1 - (NT + 1))
                wait(pe, out_added, b, t, OC, m - 1 - (NT + 1) * OC)
                cols = slice(m * P, (m + 1) * P)
                bank = out_ps[m % 2]
                nc.tensor.matmul(bank[:, :], vo_h[:, cols], pt_h[:, :], start=True, stop=False)
                nc.tensor.matmul(bank[:, :], vo_l[:, cols], pt_h[:, :], start=False, stop=False)
                nc.tensor.matmul(bank[:, :], vo_h[:, cols], pt_l[:, :], start=False, stop=True).then_inc(out_done, 1)

            def scores(b, t):
                if t == 0:
                    pe.wait_ge(key_ready, b)
                if t == 0:
                    wait(pe, q_stored, b, t, QC, 0)
                wait(pe, exp_done, b, t, 1, -NT)
                for j in range(SUB):
                    for i in range(QC):
                        last = nc.tensor.matmul(score_ps[:, j * CELLS:(j + 1) * CELLS], q[:, t, i, j * P:(j + 1) * P],
                                                key[:, i, :], start=(i == 0), stop=(i == QC - 1))
                last.then_inc(scores_done, 1)

            def project_values(b):
                pe.wait_ge(value_ready, b)
                wait(pe, pt_lo, b, 0, 1, 1 - (NT + 1))
                for m in range(VC):
                    last = nc.tensor.matmul(t_ps[0:CELLS, :], value[:, m, :], woT[:, m, :], start=(m == 0),
                                            stop=(m == VC - 1))
                last.then_inc(vo_done, 1)

            def step(b, t):
                if output(b, t):
                    turn_probs(b, t)
                for c in range(VC):
                    if convolved(b):
                        conv(b, t, c)
                    if output(b, t):
                        project(b, t, c)
                if scored(b, t) and (convolved(b) or False):
                    scores(b, t)
                elif scored(b, t):
                    scores(b, t)
                if scored(b, t) and t == 0:
                    project_values(b)
                if convolved(b):
                    for c in range(VC, CC):
                        conv(b, t, c)

            steps(pe, step)

        @block.scalar
        def _(act):
            first = 0
            for vectors, chunks in ((v_bn, VC), (qk_bn, QC), (out_bn, OC)):
                for r, vec in enumerate(vectors):
                    row = r * PAR + first
                    act.dma_start(bn_rows[row:row + chunks, :], vec.rearrange("(m p) -> m p", p=P)).then_inc(bn_in, 16)
                first += chunks
            first = 0
            for n, (w, chunks) in enumerate(((v_w, VC), (qk_w, QC), (out_w, OC))):
                act.dma_start(w_raw[:, first:first + chunks, :], w.rearrange("(m p) c -> p m c", p=P)).then_inc(w_in[n], 16)
                first += chunks

            def split_hi(b, t, part):
                i, j = slot(b, t)
                if part == 0:
                    act.wait_ge(x_in[t], (b + 1) * 16)
                    wait(act, conv_done, b, t, CC, -CC)
                    nc.scalar.activation(xh_a[:, t % 2, :, :], xr[:, i, j, 0:2, :], ACT.Copy).then_inc(x_hi, 1)
                else:
                    wait(act, late_used, b, t, 2, part - 2)
                    nc.scalar.activation(xh_b[:, part - 1, :], xr[:, i, j, part + 1, :], ACT.Copy).then_inc(x_hi, 1)

            act.wait_ge(bn_step, 2)
            nc.scalar.activation(rstd[:, :], tmp[:, :], ACT.Sqrt).then_inc(sqrt_made, 1)
            for part in range(3):
                split_hi(0, 0, part)
            for j in range(PAR):
                act.wait_ge(w_turned, j + 1)
                src = conv_ps[j % 4][:, :].rearrange("p (k n) -> p k n", k=KC)
                dst = wh[:, :, j * P:(j + 1) * P] if j < CC else woT[:, :, (j - CC) * P:(j - CC + 1) * P]
                nc.scalar.activation(dst, src, ACT.Copy).then_inc(w_hi, 1)

            def store_q(b, t, i):
                wait(act, conv_done, b, t, CC, VC + i + 1)
                bank = conv_ps[(VC + i) % 4 if t % 2 == 0 else (VC + i + 2) % 4]
                nc.scalar.activation(q[:, t, i, :], bank[:, :], ACT.Relu, bias=shift[:, VC + i:VC + i + 1])\
                    .then_inc(q_stored, 1)

            def step(b, t):
                if output(b, t):
                    wait(act, turned, b, t, 1, 1 - (NT + 1))
                    nc.scalar.activation(pt_h[:, :], t_ps[0:CELLS, :], ACT.Copy).then_inc(pt_hi, 1)
                if splits(b, t):
                    split_hi(*next_tile(b, t), 0)
                if scored(b, t):
                    wait(act, max_ready, b, t, 1, 1 - NT)
                    wait(act, turned, b, t, 1, -NT)
                    for j in range(SUB):
                        last = nc.scalar.activation(probs[:, j, :], score_ps[:, j * CELLS:(j + 1) * CELLS], ACT.Exp,
                                                    bias=neg_max[:, j:j + 1], accum_out=sums[:, j:j + 1])
                    last.then_inc(exp_done, 1)
                if scored(b, t) and t == 0:
                    act.wait_ge(vo_done, b)
                    nc.scalar.activation(vo_h[:, :], t_ps[0:CELLS, :], ACT.Copy).then_inc(vo_hi, 1)
                if convolved(b):
                    store_q(b, t, 0)
                if splits(b, t):
                    split_hi(*next_tile(b, t), 1)
                    split_hi(*next_tile(b, t), 2)
                if convolved(b):
                    store_q(b, t, 1)

            steps(act, step)

        @block.vector
        def _(dve):
            n_bn = [0]

            def bn_chain(ins):
                n_bn[0] += 1
                ins.then_inc(bn_step, 1)
                dve.wait_ge(bn_step, n_bn[0])

            GAMMA, BETA, MEAN, VAR = (bn[:, r, :] for r in range(4))
            dve.wait_ge(bn_turned, 1)
            bn_chain(nc.vector.tensor_copy(bn[:, :, :], out_ps[0][:, 0:4 * PAR].rearrange("p (r c) -> p r c", r=4)))
            bn_chain(nc.vector.tensor_scalar(tmp[:, :], VAR, EPS, None, ALU.add))
            dve.wait_ge(sqrt_made, 1)
            bn_chain(nc.vector.reciprocal(rstd[:, :], rstd[:, :]))
            bn_chain(nc.vector.tensor_tensor(tmp[:, :], tmp[:, :], rstd[:, :], ALU.mult))
            bn_chain(nc.vector.tensor_tensor(tmp[:, :], tmp[:, :], rstd[:, :], ALU.mult))
            bn_chain(nc.vector.tensor_scalar(tmp[:, :], tmp[:, :], -0.5, 1.5, ALU.mult, ALU.add))
            bn_chain(nc.vector.tensor_tensor(rstd[:, :], tmp[:, :], rstd[:, :], ALU.mult))
            bn_chain(nc.vector.tensor_tensor(scale[:, :], GAMMA, rstd[:, :], ALU.mult))
            bn_chain(nc.vector.tensor_tensor(tmp[:, :], MEAN, scale[:, :], ALU.mult))
            bn_chain(nc.vector.tensor_tensor(shift[:, :], BETA, tmp[:, :], ALU.subtract))
            for j in range(PAR):
                if j in (0, VC, CC):
                    dve.wait_ge(w_in[(0, VC, CC).index(j)], 16)
                nc.vector.tensor_scalar(w_raw[:, j, :], w_raw[:, j, :], scale[:, j:j + 1], None, ALU.mult)\
                    .then_inc(w_scaled, 1)

            def split_lo(b, t, part):
                i, j = slot(b, t)
                wait(dve, x_hi, b, t, 3, part + 1)
                if part == 0:
                    hi, lo, src = xh_a[:, t % 2, :, :], xl_a[:, t % 2, :, :], xr[:, i, j, 0:2, :]
                else:
                    hi, lo, src = xh_b[:, part - 1, :], xl_b[:, part - 1, :], xr[:, i, j, part + 1, :]
                nc.vector.tensor_tensor(lo, src, hi, ALU.subtract).then_inc(x_lo, 1)

            for j in range(CC):
                dve.wait_ge(w_hi, j + 1)
                src = conv_ps[j % 4][:, :].rearrange("p (k n) -> p k n", k=KC)
                cols = slice(j * P, (j + 1) * P)
                nc.vector.tensor_tensor(wl[:, :, cols], src, wh[:, :, cols], ALU.subtract).then_inc(w_lo, 1)
            for part in range(3):
                split_lo(0, 0, part)

            def pool_rows(b, t, c):
                if c == 0:
                    wait(dve, cells_pooled, b, t, 1, 0)
                if c < VC:
                    wait(dve, conv_done, b, t, CC, c + 1)
                    src = conv_ps[c % 4 if t % 2 == 0 else (c + 2) % 4][:, :]
                else:
                    wait(dve, q_stored, b, t, QC, c - VC + 1)
                    src = q[:, t, c - VC, :]
                for n, (r0, r1) in enumerate(ROW_PARTS[t % 4]):
                    last = nc.vector.tensor_reduce(row_max[:, c, n, :],
                                                   src[:, r0 * W:r1 * W].rearrange("p (r w) -> p w r", w=W),
                                                   AX.X, ALU.max)
                last.then_inc(rows_pooled, 1)

            def pool_cells(b, t):
                n = len(ROW_PARTS[t % 4])
                wait(dve, rows_pooled, b, t, CC, CC)
                out8 = cells[:, :, CELL8 + 8 * t:CELL8 + 8 * t + 8]
                if n == 1:
                    nc.vector.tensor_reduce(out8, row_max[:, :, 0, :].rearrange("p c (g w) -> p c g w", g=8), AX.X, ALU.max)
                else:
                    nc.vector.tensor_reduce(out8, row_max[:, :, :, :].rearrange("p c n (g w) -> p c g n w", g=8),
                                            AX.XY, ALU.max)
                halves = row_max[:, :, :, :].rearrange("p c n (g w) -> p c n g w", g=2)
                for i, (a, length) in enumerate(WINDOWS6):
                    for m in range(n):
                        last = nc.vector.tensor_reduce(part6[:, :, PART_AT[t] + m, i:i + 4:3],
                                                       halves[:, :, m, :, a:a + length], AX.X, ALU.max)
                last.then_inc(cells_pooled, 1)

            def finish_grids(b):
                wait(dve, cells_pooled, b, 0, 1, 0)
                g6 = cells[:, :, CELL6:CELL8].rearrange("p c (r w) -> p c r w", r=6)
                g3 = cells[:, :, CELL3:CELL6].rearrange("p c (r w) -> p c r w", r=3)
                nc.vector.tensor_tensor(g6, part6[:, :, 0::2, :], part6[:, :, 1::2, :], ALU.max).then_inc(grid_step, 1)
                dve.wait_ge(grid_step, b * 4 - 3)
                nc.vector.tensor_tensor(rows3[:, :, :, :], g6[:, :, 0::2, :], g6[:, :, 1::2, :], ALU.max).then_inc(grid_step, 1)
                dve.wait_ge(grid_step, b * 4 - 2)
                nc.vector.tensor_tensor(g3, rows3[:, :, :, 0::2], rows3[:, :, :, 1::2], ALU.max).then_inc(grid_step, 1)
                dve.wait_ge(grid_step, b * 4 - 1)
                nc.vector.tensor_reduce(cells[:, :, CELL1:CELL3], cells[:, :, CELL3:CELL6], AX.X, ALU.max).then_inc(grid_step, 1)
                dve.wait_ge(grid_step, b * 4)
                nc.vector.tensor_scalar(key[:, :, :], cells[:, VC:CC, :], float(CK) ** -0.5, None, ALU.mult)\
                    .then_inc(key_ready, 1)
                for m in range(VC):
                    last = nc.vector.tensor_scalar(value[:, m, :], cells[:, m, :], shift[:, m:m + 1], 0.0, ALU.add, ALU.max)
                last.then_inc(value_ready, 1)

            def add_out(b, t, m):
                wait(dve, out_done, b, t, OC, m + 1 - (NT + 1) * OC)
                i, j = slot(b, t - NT - 1)
                xt = xr[:, i, j, m, :]
                nc.vector.scalar_tensor_tensor(xt, out_ps[m % 2][:, :], shift[:, CC + m:CC + m + 1], xt,
                                               ALU.add, ALU.add).then_inc(out_added, 1)

            def step(b, t):
                has_out, has_conv, has_split = output(b, t), convolved(b), splits(b, t)
                if has_out:
                    wait(dve, pt_hi, b, t, 1, 1 - (NT + 1))
                    nc.vector.tensor_tensor(pt_l[:, :], t_ps[0:CELLS, :], pt_h[:, :], ALU.subtract).then_inc(pt_lo, 1)
                if not isinstance(b, int) or 1 <= NT * b + t <= NT * B:
                    pool_cells(*((b, t - 1) if t else (b - 1, NT - 1)))
                if t == 0 and scored(b, t):
                    finish_grids(b)
                for c in range(VC):
                    if has_conv:
                        pool_rows(b, t, c)
                    if has_out:
                        add_out(b, t, c)
                    if c == 1 and has_split:
                        split_lo(*next_tile(b, t), 0)
                if scored(b, t):
                    wait(dve, scores_done, b, t, 1, 1 - NT)
                    nc.vector.tensor_reduce(neg_max[:, :], score_ps[:, 0:SUB * CELLS].rearrange("p (j c) -> p j c", j=SUB),
                                            AX.X, ALU.max, negate=True).then_inc(max_ready, 1)
                    wait(dve, exp_done, b, t, 1, 1 - NT)
                    nc.vector.reciprocal(rsum[:, :], sums[:, :]).then_inc(rsum_ready, 1)
                    wait(dve, rsum_ready, b, t, 1, 1 - NT)
                    nc.vector.tensor_tensor(probs[:, :, :], probs[:, :, :],
                                            rsum[:, :].unsqueeze(2).broadcast_to([P, SUB, CELLS]), ALU.mult).then_inc(probs_ready, 1)
                if t == 0 and scored(b, t):
                    dve.wait_ge(vo_hi, b)
                    nc.vector.tensor_tensor(vo_l[:, :], t_ps[0:CELLS, :], vo_h[:, :], ALU.subtract).then_inc(vo_lo, 1)
                if has_conv:
                    pool_rows(b, t, VC)
                if has_split:
                    split_lo(*next_tile(b, t), 1)
                    split_lo(*next_tile(b, t), 2)
                if has_conv:
                    pool_rows(b, t, VC + 1)

            steps(dve, step)


def kernel(x, L0_conv_qk_w, L0_conv_qk_gamma, L0_conv_qk_beta, L0_conv_qk_mean, L0_conv_qk_var,
           L0_conv_v_w, L0_conv_v_gamma, L0_conv_v_beta, L0_conv_v_mean, L0_conv_v_var,
           L0_conv_out_w, L0_conv_out_gamma, L0_conv_out_beta, L0_conv_out_mean, L0_conv_out_var):
    import numpy as np
    import concourse.bacc as bacc
    from concourse.bass_utils import run_bass_kernel_spmd

    given = {
        "x": x, "qk_w": L0_conv_qk_w, "v_w": L0_conv_v_w, "out_w": L0_conv_out_w,
        "qk_gamma": L0_conv_qk_gamma, "qk_beta": L0_conv_qk_beta, "qk_mean": L0_conv_qk_mean, "qk_var": L0_conv_qk_var,
        "v_gamma": L0_conv_v_gamma, "v_beta": L0_conv_v_beta, "v_mean": L0_conv_v_mean, "v_var": L0_conv_v_var,
        "out_gamma": L0_conv_out_gamma, "out_beta": L0_conv_out_beta, "out_mean": L0_conv_out_mean,
        "out_var": L0_conv_out_var,
    }
    nc = bacc.Bacc("TRN2", target_bir_lowering=False, num_devices=1)
    arrays, aps = {}, {}
    for name, a in given.items():
        arrays[name] = np.ascontiguousarray(a)
        aps[name] = nc.dram_tensor(name, arrays[name].shape, F32, kind="ExternalInput").ap()
    out = nc.dram_tensor("out", arrays["x"].shape, F32, kind="ExternalOutput").ap()

    def bn_of(layer):
        return [aps[f"{layer}_{p}"] for p in ("gamma", "beta", "mean", "var")]

    psp_attention(nc, aps["x"], aps["qk_w"], bn_of("qk"), aps["v_w"], bn_of("v"), aps["out_w"], bn_of("out"), out)
    r = run_bass_kernel_spmd(nc, [arrays], core_ids=[0])
    return r.results[0]["out"]
```

```python
from contextlib import ExitStack

import concourse.bass as bass
from concourse import mybir
from concourse.alu_op_type import AluOpType as ALU

F32 = mybir.dt.float32
F32R = mybir.dt.float32r
ACT = mybir.ActivationFunctionType
AX = mybir.AxisListType

P = 128
EPS = 1e-5
CELL1, CELL3, CELL6, CELL8 = 0, 1, 1 + 9, 1 + 9 + 36
CELLS = 1 + 9 + 36 + 64
WINDOWS6 = [(0, 11), (10, 12), (21, 11)]
ROW_PARTS = [[(0, 8)], [(0, 3), (2, 8)], [(0, 6), (5, 8)], [(0, 8)]]
PART_AT = [0, 1, 3, 5, 6, 7, 9, 11]


def psp_attention(nc, x, qk_w, v_w, out_w, bn_in_rows, out):
    B, CIN, H, W = x.shape
    CK, CV = qk_w.shape[0], v_w.shape[0]
    NT = 8
    TN = H * W // NT
    KC = CIN // P
    VC, QC, OC = CV // P, CK // P, CIN // P
    CC = VC + QC
    SUB = TN // P
    GR = 4
    RING = 3
    assert (H, W, TN, KC, VC, QC) == (64, 64, 512, 4, 4, 2)
    PAR = CC + OC

    x_v = x.rearrange("b (k p) h w -> b p k (h w)", p=P)
    out_v = out.rearrange("b (k p) h w -> b p k (h w)", p=P)

    with ExitStack() as ctx:
        def sb(name, shape, dt=F32):
            return ctx.enter_context(nc.sbuf_tensor(name, shape, dt))

        def psum(name):
            return ctx.enter_context(nc.psum_tensor(name, [P, TN], F32))

        def sem(name):
            return ctx.enter_context(nc.semaphore(name))

        xr = sb("xr", [P, RING, GR, KC, TN])
        q = sb("q", [P, NT, QC, TN])
        w_raw = q[:, :, :, :].rearrange("p t c n -> p (t c) n")[:, NT * QC - PAR:NT * QC, :]
        xh_a = sb("xh_a", [P, 2, 2, TN], F32R)
        xl_a = sb("xl_a", [P, 2, 2, TN], F32R)
        xh_b = sb("xh_b", [P, 2, TN], F32R)
        xl_b = sb("xl_b", [P, 2, TN], F32R)
        wh = sb("wh", [P, KC, CC * P], F32R)
        wl = sb("wl", [P, KC, CC * P], F32R)
        woT = sb("woT", [P, VC, CIN])
        row_max = sb("row_max", [P, CC, 2, W])
        part6 = sb("part6", [P, CC, 12, 6])
        rows3 = sb("rows3", [P, CC, 3, 6])
        cells = sb("cells", [P, CC, CELLS])
        key = sb("key", [P, QC, CELLS])
        value = sb("value", [P, VC, CELLS])
        vo_h = sb("vo_h", [CELLS, CIN], F32R)
        vo_l = sb("vo_l", [CELLS, CIN], F32R)
        neg_max = sb("neg_max", [P, 2, SUB])
        sums = sb("sums", [P, 2, SUB])
        rsum = sb("rsum", [P, 2, SUB])
        probs = sb("probs", [P, 2, SUB, CELLS])
        pt_h = sb("pt_h", [CELLS, TN], F32R)
        pt_l = sb("pt_l", [CELLS, TN], F32R)
        ident = sb("ident", [P, P])
        bn_rows = sb("bn_rows", [4 * PAR, P])
        rstd = sb("rstd", [P, PAR])
        tmp = sb("tmp", [P, PAR])
        scale = sb("scale", [P, PAR])
        shift = sb("shift", [P, PAR])

        conv_ps = [psum(f"conv_ps{i}") for i in range(4)]
        score_ps = psum("score_ps")
        t_ps = psum("t_ps")
        out_ps = [psum(f"out_ps{i}") for i in range(2)]

        x_in = [sem(f"x_in{t}") for t in range(NT)]
        y_out = [sem(f"y_out{t}") for t in range(NT)]
        x_first = sem("x_first")
        y_last = sem("y_last")
        bn_in = sem("bn_in")
        w_in = [sem(f"w_in{i}") for i in range(VC + 2)]
        ident_made = sem("ident_made")
        bn_turned = sem("bn_turned")
        bn_step = sem("bn_step")
        sqrt_made = sem("sqrt_made")
        w_scaled = sem("w_scaled")
        w_turned = sem("w_turned")
        w_hi = sem("w_hi")
        w_lo = sem("w_lo")
        x_hi = sem("x_hi")
        x_lo = sem("x_lo")
        conv_done = sem("conv_done")
        late_used = sem("late_used")
        q_stored = sem("q_stored")
        rows_pooled = sem("rows_pooled")
        cells_pooled = sem("cells_pooled")
        grid_step = sem("grid_step")
        key_ready = sem("key_ready")
        value_ready = sem("value_ready")
        scores_done = sem("scores_done")
        max_ready = sem("max_ready")
        exp_done = sem("exp_done")
        rsum_ready = sem("rsum_ready")
        probs_ready = sem("probs_ready")
        turned = sem("turned")
        pt_hi = sem("pt_hi")
        pt_lo = sem("pt_lo")
        vo_done = sem("vo_done")
        vo_hi = sem("vo_hi")
        vo_lo = sem("vo_lo")
        out_done = sem("out_done")
        out_added = sem("out_added")

        setup_ps = [score_ps, t_ps, out_ps[0], out_ps[1]]

        def score_bank(b, t):
            return conv_ps[0] if isinstance(b, int) and b >= B and t % 2 else score_ps

        def out_bank(b, t, m):
            tail = isinstance(b, int) and b >= B
            return [*out_ps, conv_ps[1], conv_ps[2]][m] if tail else out_ps[m % 2]

        block = ctx.enter_context(nc.Block())

        def count(b, t, per, n):
            return b * (NT * per) + (t * per + n)

        def wait(eng, s, b, t, per, n):
            if not isinstance(b, int) or count(b, t, per, n) > 0:
                eng.wait_ge(s, count(b, t, per, n))

        def slot(b, t):
            return (2 * b + (t // GR) % RING) % RING, t % GR

        def scored(b):
            return not isinstance(b, int) or b >= 1

        def output(b, t):
            return not isinstance(b, int) or NT * b + t >= NT + 1

        def steps(eng, step, tail):
            for s in range(NT + 2):
                step(*divmod(s, NT))
            with eng.Fori(1, B - 1) as b:
                for s in range(2, NT + 2):
                    step(b + s // NT, s % NT)
            for s in range((B - 1) * NT + 2, B * NT):
                step(*divmod(s, NT))
            tail()

        def next_tile(b, t):
            return (b, t + 1) if t + 1 < NT else (b + 1, 0)

        def splits(b, t):
            return not isinstance(b, int) or NT * b + t + 1 < NT * B

        @block.sync
        def _(sp):
            def load(b, t, sem_t):
                i, j = slot(b, t)
                bb, tt = (b, t) if t < NT else (b + 1, t - NT)
                sp.dma_start(xr[:, i, j, :, :], x_v[bb, :, :, tt * TN:(tt + 1) * TN]).then_inc(x_in[sem_t], 16)

            def store(b, t):
                wait(sp, out_added, b, t, OC, OC - (NT + 1) * OC)
                i, j = slot(b, t - NT - 1)
                tt = (t - 1) % NT
                bb = b - 1 if t >= 1 else b - 2
                sp.dma_start(out_v[bb, :, :, tt * TN:(tt + 1) * TN], xr[:, i, j, :, :]).then_inc(y_out[tt], 16)

            sp.dma_start(bn_rows[:, :], bn_in_rows).then_inc(bn_in, 16)
            sp.dma_start(xr[:, 0, 0, 0:2, :], x_v[0, :, 0:2, 0:TN]).then_inc(x_first, 16)
            sp.dma_start(xr[:, 0, 0, 2:KC, :], x_v[0, :, 2:KC, 0:TN]).then_inc(x_in[0], 16)
            sp.dma_start(w_raw[:, VC:CC, :], qk_w.rearrange("(m p) c -> p m c", p=P)).then_inc(w_in[VC], 16)
            sp.wait_ge(w_in[VC - 1], 16)
            load(0, 1, 1)
            sp.dma_start(w_raw[:, CC:PAR, :], out_w.rearrange("(m p) c -> p m c", p=P)).then_inc(w_in[VC + 1], 16)

            def step(b, t):
                if not isinstance(b, int) or NT * b + t + 2 < NT * B:
                    n = (t + 2) % NT
                    if not isinstance(b, int) or NT * b + t + 2 >= NT:
                        sp.wait_ge(x_in[n], (b + (t + 2) // NT) * 16)
                    if isinstance(b, int):
                        wait(sp, conv_done, b, t, CC, 1 - CC)
                    if not isinstance(b, int) or NT * b + t >= NT + 2:
                        bb = b - 1 if t >= 2 else b - 2
                        sp.wait_ge(y_out[(t - 2) % NT], (bb + 1) * 16)
                    load(b, t + 2, n)
                if output(b, t):
                    store(b, t)

            def tail():
                for t in range(NT):
                    store(B, t)
                i, j = slot(B, -1)
                for m in range(OC):
                    sp.wait_ge(out_added, (B * NT - 1) * OC + m + 1)
                    sp.dma_start(out_v[B - 1, :, m, (NT - 1) * TN:], xr[:, i, j, m, :]).then_inc(y_last, 16)
                sp.wait_ge(y_last, OC * 16)

            steps(sp, step, tail)
            for t in range(NT):
                sp.wait_ge(y_out[t], (B - (t == NT - 1)) * 16)

        @block.gpsimd
        def _(pool):
            nc.gpsimd.memset(ident[:, :], 0.0).then_inc(ident_made, 1)
            pool.wait_ge(ident_made, 1)
            nc.gpsimd.affine_select(out=ident[:, :], in_=ident[:, :], compare_op=ALU.not_equal, fill=1.0, base=0,
                                    pattern=[[-1, P]], channel_multiplier=1).then_inc(ident_made, 1)

        @block.tensor
        def _(pe):
            pe.wait_ge(ident_made, 2)
            pe.wait_ge(bn_in, 16)
            nc.tensor.transpose(conv_ps[3][:, 0:4 * PAR], bn_rows[:, :], ident[0:4 * PAR, 0:4 * PAR]).then_inc(bn_turned, 1)

            def turn_weights(j):
                pe.wait_ge(w_scaled, j + 1)
                if j >= 4:
                    pe.wait_ge(w_lo, j - 3)
                for k in range(KC):
                    last = nc.tensor.transpose(setup_ps[j % 4][:, k * P:(k + 1) * P], w_raw[:, j, k * P:(k + 1) * P],
                                               ident[:, :])
                last.then_inc(w_turned, 1)

            def conv(b, t, c):
                if c < 2:
                    wait(pe, rows_pooled, b, t, CC, c + 3 - CC)
                elif c < 4:
                    wait(pe, q_stored, b, t, QC, c - 1 - QC)
                else:
                    wait(pe, rows_pooled, b, t, CC, c - 3)
                bank = conv_ps[c % 4 if t % 2 == 0 else (c + 2) % 4]
                order = range(KC) if c < CC - 1 else [2, 3, 0, 1]
                for n, k in enumerate(order):
                    if c == 0 and k != 1:
                        wait(pe, x_lo, b, t, 3, max(k, 1))
                    hi = xh_a[:, t % 2, k, :] if k < 2 else xh_b[:, k - 2, :]
                    lo = xl_a[:, t % 2, k, :] if k < 2 else xl_b[:, k - 2, :]
                    cols = slice(c * P, (c + 1) * P)
                    nc.tensor.matmul(bank[:, :], wh[:, k, cols], hi, start=(n == 0), stop=False)
                    nc.tensor.matmul(bank[:, :], wl[:, k, cols], hi, start=False, stop=False)
                    last = nc.tensor.matmul(bank[:, :], wh[:, k, cols], lo, start=False, stop=(n == KC - 1))
                    if c == CC - 1 and k >= 2:
                        last.then_inc(late_used, 1)
                last.then_inc(conv_done, 1)

            def turn_probs(b, t):
                if t == 1:
                    pe.wait_ge(vo_lo, b)
                wait(pe, probs_ready, b, t, 1, 1 - (NT + 1))
                wait(pe, pt_lo, b, t, 1, -(NT + 1))
                for j in range(SUB):
                    last = nc.tensor.transpose(t_ps[0:CELLS, j * P:(j + 1) * P], probs[:, (t + 1) % 2, j, :], ident[:, :])
                last.then_inc(turned, 1)

            def project(b, t, m):
                if m == 0:
                    wait(pe, pt_lo, b, t, 1, 1 - (NT + 1))
                four = isinstance(b, int) and NT * b + t > NT * B
                if m < 2 or four or not (isinstance(b, int) and b >= B):
                    wait(pe, out_added, b, t, OC, m - (3 if four else 1) - (NT + 1) * OC)
                cols = slice(m * P, (m + 1) * P)
                bank = out_bank(b, t, m)
                nc.tensor.matmul(bank[:, :], vo_h[:, cols], pt_h[:, :], start=True, stop=False)
                nc.tensor.matmul(bank[:, :], vo_l[:, cols], pt_h[:, :], start=False, stop=False)
                nc.tensor.matmul(bank[:, :], vo_h[:, cols], pt_l[:, :], start=False, stop=True).then_inc(out_done, 1)

            def scores(b, t):
                if t == 0:
                    pe.wait_ge(key_ready, b)
                if t == 0:
                    wait(pe, q_stored, b, t, QC, 0)
                two = isinstance(b, int) and NT * b + t > NT * B
                wait(pe, exp_done, b, t, 1, -NT - two)
                bank = score_bank(b, t)
                for j in range(SUB):
                    for i in range(QC):
                        last = nc.tensor.matmul(bank[:, j * CELLS:(j + 1) * CELLS], q[:, t, i, j * P:(j + 1) * P],
                                                key[:, i, :], start=(i == 0), stop=(i == QC - 1))
                last.then_inc(scores_done, 1)

            def project_values(b):
                pe.wait_ge(value_ready, b)
                wait(pe, pt_lo, b, 0, 1, 1 - (NT + 1))
                for m in range(VC):
                    last = nc.tensor.matmul(t_ps[0:CELLS, :], value[:, m, :], woT[:, m, :], start=(m == 0),
                                            stop=(m == VC - 1))
                last.then_inc(vo_done, 1)

            def step(b, t):
                first = isinstance(b, int) and NT * b + t == 0
                if isinstance(b, int) and NT * b + t == 1:
                    for j in range(CC, PAR):
                        turn_weights(j)
                if output(b, t):
                    turn_probs(b, t)
                for c in range(VC):
                    if first:
                        for j in ([2], [3, 4], [5])[c - 1] if c else []:
                            turn_weights(j)
                        pe.wait_ge(w_lo, c + 1)
                    conv(b, t, c)
                    if output(b, t):
                        project(b, t, c)
                if scored(b):
                    if isinstance(b, int) and NT * b + t == NT:
                        pe.wait_ge(w_hi, PAR)
                    scores(b, t)
                    if t == 0:
                        project_values(b)
                for c in range(VC, CC):
                    if first:
                        pe.wait_ge(w_lo, c + 1)
                    conv(b, t, c)

            def tail():
                turn_probs(B, 0)
                for m in range(OC):
                    if m == 2:
                        pe.wait_ge(rows_pooled, B * NT * CC - QC)
                        pe.wait_ge(q_stored, B * NT * QC)
                    project(B, 0, m)
                scores(B, 0)
                scores(B, 1)
                project_values(B)
                for t in range(1, NT + 1):
                    turn_probs(B, t)
                    if t + 1 < NT:
                        scores(B, t + 1)
                    for m in range(OC):
                        project(B, t, m)

            turn_weights(0)
            turn_weights(1)
            steps(pe, step, tail)

        @block.scalar
        def _(act):
            for m in range(VC):
                act.dma_start(w_raw[:, m, :], v_w[m * P:(m + 1) * P, :]).then_inc(w_in[m], 16)

            def split_hi(b, t, part):
                i, j = slot(b, t)
                if part == 0:
                    if isinstance(b, int) and NT * b + t == 0:
                        act.wait_ge(x_first, 16)
                    else:
                        act.wait_ge(x_in[t], (b + 1) * 16)
                    wait(act, conv_done, b, t, CC, -CC)
                    nc.scalar.activation(xh_a[:, t % 2, :, :], xr[:, i, j, 0:2, :], ACT.Copy).then_inc(x_hi, 1)
                else:
                    wait(act, late_used, b, t, 2, part - 2)
                    nc.scalar.activation(xh_b[:, part - 1, :], xr[:, i, j, part + 1, :], ACT.Copy).then_inc(x_hi, 1)

            def weights_hi(j):
                act.wait_ge(w_turned, j + 1)
                src = setup_ps[j % 4][:, :].rearrange("p (k n) -> p k n", k=KC)
                dst = wh[:, :, j * P:(j + 1) * P] if j < CC else woT[:, :, (j - CC) * P:(j - CC + 1) * P]
                nc.scalar.activation(dst, src, ACT.Copy).then_inc(w_hi, 1)

            act.wait_ge(bn_step, 1)
            nc.scalar.activation(rstd[:, :], tmp[:, :], ACT.Sqrt).then_inc(sqrt_made, 1)
            split_hi(0, 0, 0)
            weights_hi(0)
            act.wait_ge(x_in[0], 16)
            split_hi(0, 0, 1)
            split_hi(0, 0, 2)
            for j in range(1, CC):
                weights_hi(j)

            def store_q(b, t, i):
                wait(act, conv_done, b, t, CC, VC + i + 1)
                bank = conv_ps[(VC + i) % 4 if t % 2 == 0 else (VC + i + 2) % 4]
                nc.scalar.activation(q[:, t, i, :], bank[:, :], ACT.Relu, bias=shift[:, VC + i:VC + i + 1])\
                    .then_inc(q_stored, 1)

            def probs_hi(b, t):
                wait(act, turned, b, t, 1, 1 - (NT + 1))
                nc.scalar.activation(pt_h[:, :], t_ps[0:CELLS, :], ACT.Copy).then_inc(pt_hi, 1)

            def exps(b, t):
                wait(act, max_ready, b, t, 1, 1 - NT)
                wait(act, turned, b, t, 1, -NT - 1)
                bank = score_bank(b, t)
                for j in range(SUB):
                    last = nc.scalar.activation(probs[:, t % 2, j, :], bank[:, j * CELLS:(j + 1) * CELLS], ACT.Exp,
                                                bias=neg_max[:, t % 2, j:j + 1], accum_out=sums[:, t % 2, j:j + 1])
                last.then_inc(exp_done, 1)

            def values_hi(b):
                act.wait_ge(vo_done, b)
                nc.scalar.activation(vo_h[:, :], t_ps[0:CELLS, :], ACT.Copy).then_inc(vo_hi, 1)

            def step(b, t):
                if isinstance(b, int) and NT * b + t == 1:
                    for j in range(CC, PAR):
                        weights_hi(j)
                if output(b, t):
                    probs_hi(b, t)
                if splits(b, t):
                    split_hi(*next_tile(b, t), 0)
                if scored(b):
                    exps(b, t)
                    if t == 0:
                        values_hi(b)
                store_q(b, t, 0)
                if splits(b, t):
                    split_hi(*next_tile(b, t), 1)
                    split_hi(*next_tile(b, t), 2)
                store_q(b, t, 1)

            def tail():
                probs_hi(B, 0)
                exps(B, 0)
                exps(B, 1)
                values_hi(B)
                for t in range(1, NT + 1):
                    probs_hi(B, t)
                    if t + 1 < NT:
                        exps(B, t + 1)

            steps(act, step, tail)

        @block.vector
        def _(dve):
            n_bn = [0]

            def bn_chain(ins):
                n_bn[0] += 1
                ins.then_inc(bn_step, 1)
                dve.wait_ge(bn_step, n_bn[0])

            GAMMA, BETA, MEAN, VAR = (conv_ps[3][:, r * PAR:(r + 1) * PAR] for r in range(4))
            dve.wait_ge(bn_turned, 1)
            bn_chain(nc.vector.tensor_scalar(tmp[:, :], VAR, EPS, None, ALU.add))
            dve.wait_ge(sqrt_made, 1)
            bn_chain(nc.vector.reciprocal(rstd[:, :], rstd[:, :]))
            bn_chain(nc.vector.tensor_tensor(tmp[:, :], tmp[:, :], rstd[:, :], ALU.mult))
            bn_chain(nc.vector.scalar_tensor_tensor(tmp[:, :], tmp[:, :], -0.5, rstd[:, :], ALU.mult, ALU.mult))
            bn_chain(nc.vector.scalar_tensor_tensor(rstd[:, :], tmp[:, :], 1.5, rstd[:, :], ALU.add, ALU.mult))
            bn_chain(nc.vector.tensor_tensor(scale[:, :], GAMMA, rstd[:, :], ALU.mult))

            def scale_weights(j):
                dve.wait_ge(w_in[j if j < VC else VC if j < CC else VC + 1], 16)
                nc.vector.tensor_scalar(w_raw[:, j, :], w_raw[:, j, :], scale[:, j:j + 1], None, ALU.mult)\
                    .then_inc(w_scaled, 1)

            def split_lo(b, t, part):
                i, j = slot(b, t)
                wait(dve, x_hi, b, t, 3, part + 1)
                if part == 0:
                    hi, lo, src = xh_a[:, t % 2, :, :], xl_a[:, t % 2, :, :], xr[:, i, j, 0:2, :]
                else:
                    hi, lo, src = xh_b[:, part - 1, :], xl_b[:, part - 1, :], xr[:, i, j, part + 1, :]
                nc.vector.tensor_tensor(lo, src, hi, ALU.subtract).then_inc(x_lo, 1)

            def weights_lo(j):
                dve.wait_ge(w_hi, j + 1)
                src = setup_ps[j % 4][:, :].rearrange("p (k n) -> p k n", k=KC)
                cols = slice(j * P, (j + 1) * P)
                nc.vector.tensor_tensor(wl[:, :, cols], src, wh[:, :, cols], ALU.subtract).then_inc(w_lo, 1)

            scale_weights(0)
            bn_chain(nc.vector.tensor_tensor(tmp[:, :], MEAN, scale[:, :], ALU.mult))
            nc.vector.tensor_tensor(shift[:, :], BETA, tmp[:, :], ALU.subtract).then_inc(bn_step, 1)
            split_lo(0, 0, 0)
            weights_lo(0)
            scale_weights(1)
            split_lo(0, 0, 1)
            split_lo(0, 0, 2)
            weights_lo(1)
            scale_weights(2)
            scale_weights(3)
            for j in range(VC, CC):
                scale_weights(j)
                weights_lo(j - 2)
            weights_lo(CC - 2)
            weights_lo(CC - 1)

            def pool_rows(b, t, c):
                if c == 0:
                    wait(dve, cells_pooled, b, t, 1, 0)
                if c < VC:
                    wait(dve, conv_done, b, t, CC, c + 1)
                    src = conv_ps[c % 4 if t % 2 == 0 else (c + 2) % 4][:, :]
                else:
                    wait(dve, q_stored, b, t, QC, c - VC + 1)
                    src = q[:, t, c - VC, :]
                for n, (r0, r1) in enumerate(ROW_PARTS[t % 4]):
                    last = nc.vector.tensor_reduce(row_max[:, c, n, :],
                                                   src[:, r0 * W:r1 * W].rearrange("p (r w) -> p w r", w=W),
                                                   AX.X, ALU.max)
                last.then_inc(rows_pooled, 1)

            def pool_cells(b, t):
                n = len(ROW_PARTS[t % 4])
                wait(dve, rows_pooled, b, t, CC, CC)
                out8 = cells[:, :, CELL8 + 8 * t:CELL8 + 8 * t + 8]
                if n == 1:
                    nc.vector.tensor_reduce(out8, row_max[:, :, 0, :].rearrange("p c (g w) -> p c g w", g=8), AX.X, ALU.max)
                else:
                    nc.vector.tensor_reduce(out8, row_max[:, :, :, :].rearrange("p c n (g w) -> p c g n w", g=8),
                                            AX.XY, ALU.max)
                halves = row_max[:, :, :, :].rearrange("p c n (g w) -> p c n g w", g=2)
                for i, (a, length) in enumerate(WINDOWS6):
                    for m in range(n):
                        last = nc.vector.tensor_reduce(part6[:, :, PART_AT[t] + m, i:i + 4:3],
                                                       halves[:, :, m, :, a:a + length], AX.X, ALU.max)
                last.then_inc(cells_pooled, 1)

            def finish_grids(b):
                wait(dve, cells_pooled, b, 0, 1, 0)
                g6 = cells[:, :, CELL6:CELL8].rearrange("p c (r w) -> p c r w", r=6)
                g3 = cells[:, :, CELL3:CELL6].rearrange("p c (r w) -> p c r w", r=3)
                nc.vector.tensor_tensor(g6, part6[:, :, 0::2, :], part6[:, :, 1::2, :], ALU.max).then_inc(grid_step, 1)
                dve.wait_ge(grid_step, b * 4 - 3)
                nc.vector.tensor_tensor(rows3[:, :, :, :], g6[:, :, 0::2, :], g6[:, :, 1::2, :], ALU.max).then_inc(grid_step, 1)
                dve.wait_ge(grid_step, b * 4 - 2)
                nc.vector.tensor_tensor(g3, rows3[:, :, :, 0::2], rows3[:, :, :, 1::2], ALU.max).then_inc(grid_step, 1)
                dve.wait_ge(grid_step, b * 4 - 1)
                nc.vector.tensor_reduce(cells[:, :, CELL1:CELL3], cells[:, :, CELL3:CELL6], AX.X, ALU.max).then_inc(grid_step, 1)
                dve.wait_ge(grid_step, b * 4)
                nc.vector.tensor_scalar(key[:, :, :], cells[:, VC:CC, :], float(CK) ** -0.5, None, ALU.mult)\
                    .then_inc(key_ready, 1)
                for m in range(VC):
                    last = nc.vector.tensor_scalar(value[:, m, :], cells[:, m, :], shift[:, m:m + 1], 0.0, ALU.add, ALU.max)
                last.then_inc(value_ready, 1)

            def add_out(b, t, m):
                wait(dve, out_done, b, t, OC, m + 1 - (NT + 1) * OC)
                i, j = slot(b, t - NT - 1)
                xt = xr[:, i, j, m, :]
                nc.vector.scalar_tensor_tensor(xt, out_bank(b, t, m)[:, :], shift[:, CC + m:CC + m + 1], xt,
                                               ALU.add, ALU.add).then_inc(out_added, 1)

            def probs_lo(b, t):
                wait(dve, pt_hi, b, t, 1, 1 - (NT + 1))
                nc.vector.tensor_tensor(pt_l[:, :], t_ps[0:CELLS, :], pt_h[:, :], ALU.subtract).then_inc(pt_lo, 1)

            def maxima(b, t):
                wait(dve, scores_done, b, t, 1, 1 - NT)
                bank = score_bank(b, t)
                nc.vector.tensor_reduce(neg_max[:, t % 2, :], bank[:, 0:SUB * CELLS].rearrange("p (j c) -> p j c", j=SUB),
                                        AX.X, ALU.max, negate=True).then_inc(max_ready, 1)

            def normalise(b, t):
                wait(dve, exp_done, b, t, 1, 1 - NT)
                nc.vector.reciprocal(rsum[:, t % 2, :], sums[:, t % 2, :]).then_inc(rsum_ready, 1)
                wait(dve, rsum_ready, b, t, 1, 1 - NT)
                nc.vector.tensor_tensor(probs[:, t % 2, :, :], probs[:, t % 2, :, :],
                                        rsum[:, t % 2, :].unsqueeze(2).broadcast_to([P, SUB, CELLS]), ALU.mult)\
                    .then_inc(probs_ready, 1)

            def values_lo(b):
                dve.wait_ge(vo_hi, b)
                nc.vector.tensor_tensor(vo_l[:, :], t_ps[0:CELLS, :], vo_h[:, :], ALU.subtract).then_inc(vo_lo, 1)

            def step(b, t):
                has_out, has_split = output(b, t), splits(b, t)
                if has_out:
                    probs_lo(b, t)
                if not isinstance(b, int) or NT * b + t >= 1:
                    pool_cells(*((b, t - 1) if t else (b - 1, NT - 1)))
                if scored(b) and t == 0:
                    finish_grids(b)
                for c in range(VC):
                    pool_rows(b, t, c)
                    if has_out:
                        add_out(b, t, c)
                    if c == 1 and has_split:
                        split_lo(*next_tile(b, t), 0)
                if isinstance(b, int) and NT * b + t == 0:
                    for j in range(CC, PAR):
                        scale_weights(j)
                if scored(b):
                    maxima(b, t)
                    normalise(b, t)
                    if t == 0:
                        values_lo(b)
                pool_rows(b, t, VC)
                if has_split:
                    split_lo(*next_tile(b, t), 1)
                    split_lo(*next_tile(b, t), 2)
                pool_rows(b, t, VC + 1)

            def tail():
                probs_lo(B, 0)
                pool_cells(B - 1, NT - 1)
                finish_grids(B)
                for m in range(OC):
                    add_out(B, 0, m)
                maxima(B, 0)
                maxima(B, 1)
                normalise(B, 0)
                values_lo(B)
                for t in range(1, NT + 1):
                    probs_lo(B, t)
                    if t < NT:
                        normalise(B, t)
                    if t + 1 < NT:
                        maxima(B, t + 1)
                    for m in range(OC):
                        add_out(B, t, m)

            steps(dve, step, tail)


def kernel(x, L0_conv_qk_w, L0_conv_qk_gamma, L0_conv_qk_beta, L0_conv_qk_mean, L0_conv_qk_var,
           L0_conv_v_w, L0_conv_v_gamma, L0_conv_v_beta, L0_conv_v_mean, L0_conv_v_var,
           L0_conv_out_w, L0_conv_out_gamma, L0_conv_out_beta, L0_conv_out_mean, L0_conv_out_var):
    import numpy as np
    import concourse.bacc as bacc
    from concourse.bass_utils import run_bass_kernel_spmd

    bn = np.concatenate([
        L0_conv_v_gamma, L0_conv_qk_gamma, L0_conv_out_gamma, L0_conv_v_beta, L0_conv_qk_beta, L0_conv_out_beta,
        L0_conv_v_mean, L0_conv_qk_mean, L0_conv_out_mean, L0_conv_v_var, L0_conv_qk_var, L0_conv_out_var,
    ]).reshape(-1, P)
    given = {"x": x, "qk_w": L0_conv_qk_w, "v_w": L0_conv_v_w, "out_w": L0_conv_out_w, "bn_params": bn}
    nc = bacc.Bacc("TRN2", target_bir_lowering=False, num_devices=1)
    arrays, aps = {}, {}
    for name, a in given.items():
        arrays[name] = np.ascontiguousarray(a)
        aps[name] = nc.dram_tensor(name, arrays[name].shape, F32, kind="ExternalInput").ap()
    out = nc.dram_tensor("out", arrays["x"].shape, F32, kind="ExternalOutput").ap()

    psp_attention(nc, aps["x"], aps["qk_w"], aps["v_w"], aps["out_w"], aps["bn_params"], out)
    r = run_bass_kernel_spmd(nc, [arrays], core_ids=[0])
    return r.results[0]["out"]
```
